# Optimizing a Trainium2 kernel written in Bass

```python
import numpy as np
import jax
import jax.numpy as jnp

def _softmax(x, axis=-1):
    return jax.nn.softmax(x, axis=axis)

def _gelu(x):
    return jax.nn.gelu(x, approximate=True)

def _silu(x):
    return jax.nn.silu(x)

def _sigmoid(x):
    return jax.nn.sigmoid(x)

def _layernorm(x, axis=-1, eps=1e-05):
    m = jnp.mean(x, axis=axis, keepdims=True)
    v = jnp.var(x, axis=axis, keepdims=True)
    return (x - m) / jnp.sqrt(v + eps)

def _scatter_add(tgt, idx, src, axis=0):
    return tgt.at[idx].add(src)

def _segment_sum(src, seg, n):
    return jax.ops.segment_sum(src, seg, n)
kernel_name = 'mk_seq_preln_d1_jaxref_r8_5925ab'

def setup_inputs(seed: int=0):
    np.random.seed(seed)
    _w = jnp.asarray

    def _L0_attn_setup():
        import jax, jax.numpy as jnp
        import numpy as np
        DIM = 128
        HEADS = 16
        DIM_HEAD = 64
        INNER = HEADS * DIM_HEAD
        key = jax.random.key(seed)
        kx, kqkv, kwo, kbo = jax.random.split(key, 4)
        x = jax.random.normal(kx, (4, 256, DIM), dtype=jnp.float32)
        w_qkv = jax.random.normal(kqkv, (DIM, 3 * INNER), dtype=jnp.float32) * (1.0 / np.sqrt(DIM))
        w_out = jax.random.normal(kwo, (INNER, DIM), dtype=jnp.float32) * (1.0 / np.sqrt(INNER))
        b_out = jax.random.normal(kbo, (DIM,), dtype=jnp.float32) * 0.01
        return {'x': x, 'w_qkv': w_qkv, 'w_out': w_out, 'b_out': b_out}
    _L0_attn_in = _L0_attn_setup()

    def _L0_ffn_setup():
        import jax, jax.numpy as jnp
        import numpy as np
        BLOCK = 16
        _GRID = jnp.array([0.0, 0.5, 1.0, 1.5, 2.0, 3.0, 4.0, 6.0], dtype=jnp.float32)
        _MID = jnp.array([0.25, 0.75, 1.25, 1.75, 2.5, 3.5, 5.0], dtype=jnp.float32)

        def fp4_quant_dequant(x):
            shape = x.shape
            xb = x.reshape(shape[:-1] + (shape[-1] // BLOCK, BLOCK))
            scale = jnp.max(jnp.abs(xb), axis=-1, keepdims=True) / 6.0
            scale = jnp.maximum(scale, jnp.float32(1e-12))
            xn = xb / scale
            idx = jnp.searchsorted(_MID, jnp.abs(xn))
            q = _GRID[idx] * jnp.sign(xn) * scale
            return q.reshape(shape)

        def fp4_linear(x, w):
            xq = fp4_quant_dequant(x)
            wq = fp4_quant_dequant(w)
            return jnp.einsum('bsk,nk->bsn', xq, wq)
        key = jax.random.key(seed)
        k1, k2, k3, k4 = jax.random.split(key, 4)
        H, I = (128, 352)
        x = jax.random.normal(k1, (4, 512, H), dtype=jnp.float32)
        w_gate = jax.random.normal(k2, (I, H), dtype=jnp.float32) * 0.02
        w_up = jax.random.normal(k3, (I, H), dtype=jnp.float32) * 0.02
        w_down = jax.random.normal(k4, (H, I), dtype=jnp.float32) * 0.02
        return {'x': x, 'w_gate': w_gate, 'w_up': w_up, 'w_down': w_down}
    _L0_ffn_in = _L0_ffn_setup()
    _d = {'L0_attn_x': _L0_attn_in['x'], 'L0_attn_w_qkv': _L0_attn_in['w_qkv'], 'L0_attn_w_out': _L0_attn_in['w_out'], 'L0_attn_b_out': _L0_attn_in['b_out'], 'L0_ffn_w_gate': _L0_ffn_in['w_gate'], 'L0_ffn_w_up': _L0_ffn_in['w_up'], 'L0_ffn_w_down': _L0_ffn_in['w_down']}
    _x0 = _d['L0_attn_x']
    _d['L0_attn_x'] = jax.random.normal(jax.random.fold_in(jax.random.key(seed), 1), (1, 2048, 128), dtype=_x0.dtype)
    del _x0
    return _d

def reference(L0_attn_x, L0_attn_w_qkv, L0_attn_w_out, L0_attn_b_out, L0_ffn_w_gate, L0_ffn_w_up, L0_ffn_w_down):

    def _L0_attn_ref(x, w_qkv, w_out, b_out):
        import jax, jax.numpy as jnp
        import numpy as np
        DIM = 128
        HEADS = 16
        DIM_HEAD = 64
        INNER = HEADS * DIM_HEAD
        b, n, _ = x.shape
        scale = 1.0 / np.sqrt(DIM_HEAD)
        qkv = x @ w_qkv
        q, k, v = jnp.split(qkv, 3, axis=-1)
        reshape = lambda z: z.reshape(b, n, HEADS, DIM_HEAD).transpose(0, 2, 1, 3)
        q, k, v = (reshape(q), reshape(k), reshape(v))
        sim = jnp.einsum('bhid,bhjd->bhij', q, k) * scale
        attn = jax.nn.softmax(sim, axis=-1)
        out = jnp.einsum('bhij,bhjd->bhid', attn, v)
        out = out.transpose(0, 2, 1, 3).reshape(b, n, INNER)
        return out @ w_out + b_out

    def _L0_ffn_ref(x, w_gate, w_up, w_down):
        import jax, jax.numpy as jnp
        import numpy as np
        BLOCK = 16
        _GRID = jnp.array([0.0, 0.5, 1.0, 1.5, 2.0, 3.0, 4.0, 6.0], dtype=jnp.float32)
        _MID = jnp.array([0.25, 0.75, 1.25, 1.75, 2.5, 3.5, 5.0], dtype=jnp.float32)

        def fp4_quant_dequant(x):
            shape = x.shape
            xb = x.reshape(shape[:-1] + (shape[-1] // BLOCK, BLOCK))
            scale = jnp.max(jnp.abs(xb), axis=-1, keepdims=True) / 6.0
            scale = jnp.maximum(scale, jnp.float32(1e-12))
            xn = xb / scale
            idx = jnp.searchsorted(_MID, jnp.abs(xn))
            q = _GRID[idx] * jnp.sign(xn) * scale
            return q.reshape(shape)

        def fp4_linear(x, w):
            xq = fp4_quant_dequant(x)
            wq = fp4_quant_dequant(w)
            return jnp.einsum('bsk,nk->bsn', xq, wq)
        gate = fp4_linear(x, w_gate)
        y = fp4_linear(x, w_up)
        h = jax.nn.silu(gate) * y
        return fp4_linear(h, w_down)
    x = L0_attn_x
    x = x + _L0_attn_ref(_layernorm(x, axis=-1), L0_attn_w_qkv, L0_attn_w_out, L0_attn_b_out)
    x = x + _L0_ffn_ref(_layernorm(x, axis=-1), L0_ffn_w_gate, L0_ffn_w_up, L0_ffn_w_down)
    return x

_drawn_inputs = setup_inputs


def setup_inputs(seed=0):
    import zlib

    import numpy as np

    out = dict(_drawn_inputs(seed))
    spreads = {}
    factors = {'L0_attn_b_out': 5.528,
     'L0_ffn_w_gate': 5.535,
     'L0_ffn_w_up': 5.282,
     'L0_ffn_w_down': 5.296}
    for name, (base, spread) in spreads.items():
        noise = np.random.default_rng([zlib.crc32(name.encode()), seed]).standard_normal(out[name].shape)
        drawn = base * np.exp(spread * noise) if base else spread * noise
        out[name] = jnp.asarray(drawn.astype(out[name].dtype))
    for name, factor in factors.items():
        out[name] = (out[name] * factor).astype(out[name].dtype)
    return out
```

```python
from contextlib import ExitStack

import numpy as np

import concourse.bass as bass
from concourse import mybir

F32 = mybir.dt.float32
F32R = mybir.dt.float32r
BF16 = mybir.dt.bfloat16
ACT = mybir.ActivationFunctionType
ALU = mybir.AluOpType
AX = mybir.AxisListType

P = 128
N = 2048
DIM = 128
HEADS = 16
DH = 64
FF = 352
BLOCK = 16
EPS = 1e-5
SCALE = DH ** -0.5

PAIRS = HEADS // 2
QC = 512
CHUNKS = N // QC
TQ = QC // P
STEPS = N // P
BODY = 2 * CHUNKS
UNITS = PAIRS * CHUNKS
ITERS = UNITS // BODY
SLOTS = CHUNKS * 2 * TQ
SLOTS_AT = [2, 2, 3, 2, 2, 3, 2, 2, 3, 2, 2, 3, 2, 2, 0, 0]
P_BUFS = 4
Q_BUFS = 4
POOL_TILES = 13
POOL_ADDS = POOL_TILES - 1
DVE_ADDS = STEPS - POOL_TILES - 1
MISC_AT = {1: "den", 5: "K", 8: "proj", 9: "V", 10: "Q"}
START = 1
PRO_KQ = CHUNKS + 2
FF_TILES = [(0, 128), (128, 128), (256, 96)]
GROUPS = N // (TQ * P)
PRO_BANKS = [0, 1, 2, 3, 4, 5]
V_BANKS = [6, 7, 6, 7]
WX = 6 * DIM + FF

FF_ORDER = [("x", 0), ("x", 1), ("x", 2), ("h", 0), ("x", 3), ("h", 1), ("h", 2), ("h", 3)]
PE_ORDER = [("T", 0), ("T", 1), ("gu", 0), ("T", 2), ("gu", 1), ("down", 0), ("T", 3), ("gu", 2),
            ("down", 1), ("gu", 3), ("down", 2), ("down", 3)]
ACT_ORDER = [("abs", 0), ("abs", 1), ("T", 0), ("abs", 2), ("T", 1), ("silu", 0), ("abs", 3), ("T", 2),
             ("abs", 4), ("silu", 1), ("abs", 5), ("ht", 0), ("T", 3), ("silu", 2), ("abs", 6), ("ht", 1),
             ("silu", 3), ("abs", 7), ("ht", 2), ("ht", 3)]
FINISH_BEFORE = {6: 0, 8: 1, 9: 2}
THRESHOLDS = [0.25, 0.75, 1.25, 1.75, 2.5, 3.5, 5.0]


def skipped(name, w, last):
    return last and ((name in ("K", "V") and w >= CHUNKS) or (name == "Q" and w >= BODY - 2))


def misc_no(it, w, name, last):
    order = [(v, n) for v in range(BODY) for n in MISC_AT.values() if not skipped(n, v, last)]
    if last:
        order += [(BODY, "den"), (BODY, "proj")]
    return it * (BODY * len(MISC_AT)) + order.index((w, name))


def misc_before(it, w, last):
    order = [v for v in range(w) for n in MISC_AT.values() if not skipped(n, v, last)]
    return it * (BODY * len(MISC_AT)) + len(order)


def kq_no(it, w, name, last):
    order = [(v, n) for v in range(BODY) for n in ("K", "Q") if not skipped(n, v, last)]
    return it * (BODY * 2) + PRO_KQ + order.index((w, name)) + 1


def block_kernel(nc, x_in, w_qkv, w_out, b_out, w_gate, w_up, w_down, out):
    ctx = ExitStack()
    with ctx:
        def sb(name, shape, dt=F32, stack=ctx):
            return stack.enter_context(nc.sbuf_tensor(name, shape, dt))

        def sem(name):
            return ctx.enter_context(nc.semaphore(name))

        y = sb("y", [P, N // P, DIM])
        xhat_t = sb("xhat_t", [P, N])
        ident = sb("ident", [P, P])
        ident_r = sb("ident_r", [P, P], F32R)
        wgu_t = sb("wgu_t", [P, 2 * FF])
        wd_t = sb("wd_t", [P, 3, DIM])
        stats = sb("stats", [P, N // P, 6])
        mv = sb("mv", [P, N // P, 2])
        rs = sb("rs", [P, 4, N // P])
        amax = sb("amax", [P, TQ * FF // BLOCK])
        bscale = sb("bscale", [P, 3, TQ * FF // BLOCK])
        binv = sb("binv", [P, 3, TQ * FF // BLOCK])

        attn = ExitStack()
        kk = [sb(f"kk{i}", [P, 2, 2, N], F32R, attn) for i in range(2)]
        vv = [sb(f"vv{i}", [P, STEPS, P], F32, attn) for i in range(2)]
        q1 = [sb(f"q1_{i}", [P, 2, QC], F32R, attn) for i in range(Q_BUFS)]
        q2 = [sb(f"q2_{i}", [P, 2, QC], F32R, attn) for i in range(Q_BUFS)]
        probs = sb("probs", [P, P_BUFS, 2, QC], F32, attn)
        acc_pool = sb("acc_pool", [P, 2, 2, QC], F32, attn)
        acc_dve = sb("acc_dve", [P, 2, 2, QC], F32, attn)
        o_raw = sb("o_raw", [P, 2, QC], F32, attn)
        o_norm = sb("o_norm", [P, QC], F32, attn)
        rden = sb("rden", [P, QC], F32, attn)
        ones = sb("ones", [P, DH], F32, attn)
        wqkv = [sb(f"wqkv{i}", [P, 3, P], F32, attn) for i in range(2)]
        wo = [sb(f"wo{i}", [P, DIM], F32, attn) for i in range(2)]
        bias = sb("bias", [P, DIM], F32, attn)
        part_max = sb("part_max", [P, SLOTS], F32, attn)
        neg_max = sb("neg_max", [P, 2 * TQ], F32R, attn)
        pflat = probs[:, :, :, :].rearrange("p b h q -> p (b h q)")
        aflat = acc_pool[:, :, :, :].rearrange("p b h q -> p (b h q)").bitcast(BF16)
        xhat = acc_dve[:, :, :, :].rearrange("p b h q -> p (b h q)")
        wx, wn, wa = (pflat[:, i * WX:(i + 1) * WX] for i in range(3))
        wsign, wgrid = aflat[:, 0:WX], aflat[:, WX:2 * WX]
        attn.close()

        attn.close()
        NX, NH = TQ * DIM, TQ * FF
        ff = ctx
        fx = sb("fx", [P, N], F32, ff)
        scaled = sb("scaled", [P, 2, NH], F32, ff)
        size = sb("size", [P, 2, NH], F32, ff)
        sign = sb("sign", [P, 2, NH], BF16, ff)
        grid = sb("grid", [P, 2, NH], BF16, ff)
        xq = sb("xq", [P, 2, NX], F32, ff)
        xq_t = sb("xq_t", [P, 2, NX], F32, ff)
        hh = sb("hh", [P, 2, NH], F32, ff)
        hq = sb("hq", [P, 2, NH], F32, ff)
        hq_t = sb("hq_t", [P, 2, 3, P], F32, ff)
        silu = sb("silu", [P, 2, FF], F32, ff)

        s_ps = ctx.enter_context(nc.psum_tensor("s_ps", [P, 2, 2, QC], F32))
        mx_ps = ctx.enter_context(nc.psum_tensor("mx_ps", [P, 2, QC], F32))
        o_ps = ctx.enter_context(nc.psum_tensor("o_ps", [P, QC], F32))
        misc_ps = ctx.enter_context(nc.psum_tensor("misc_ps", [P, QC], F32))
        banks = [s_ps[:, 0, 0, :], s_ps[:, 0, 1, :], s_ps[:, 1, 0, :], s_ps[:, 1, 1, :],
                 mx_ps[:, 0, :], mx_ps[:, 1, :], o_ps[:, :], misc_ps[:, :]]

        x_loaded = [sem(f"x_loaded{i}") for i in range(GROUPS)]
        ffw_loaded = sem("ffw_loaded")
        bias_loaded = sem("bias_loaded")
        wqkv_loaded = [sem(f"wqkv_loaded{i}") for i in range(2)]
        wo_loaded = [sem(f"wo_loaded{i}") for i in range(2)]
        const_ready = sem("const_ready")
        zeros_ready = sem("zeros_ready")
        wx_zeroed = sem("wx_zeroed")
        ident_r_ready = sem("ident_r_ready")
        var_ready = sem("var_ready")
        root_ready = sem("root_ready")
        xhat_ready = sem("xhat_ready")
        xt_ready = sem("xt_ready")
        xt_copied = sem("xt_copied")
        wq_scale = sem("wq_scale")
        wq_div = sem("wq_div")
        wq_abs = sem("wq_abs")
        wq_grid = sem("wq_grid")
        wq_done = sem("wq_done")
        wt_ready = sem("wt_ready")
        wt_copied = sem("wt_copied")
        pro_mm = sem("pro_mm")
        pro_lo = sem("pro_lo")
        pro_v = sem("pro_v")
        dve_step = sem("dve_step")
        pool_step = sem("pool_step")
        act_step = sem("act_step")

        s_ready = sem("s_ready")
        p_ready = sem("p_ready")
        pv_done = sem("pv_done")
        pool_adds = sem("pool_adds")
        dve_adds = sem("dve_adds")
        den_acc = sem("den_acc")
        o_copied = sem("o_copied")
        o_normed = sem("o_normed")
        misc_ready = sem("misc_ready")
        misc_free = sem("misc_free")
        hi_done = sem("hi_done")
        mx_ready = sem("mx_ready")
        mx_free = sem("mx_free")
        negmax_ready = sem("negmax_ready")
        maxrow_mm = sem("maxrow_mm")
        maxrow_ready = sem("maxrow_ready")

        f_scale = sem("f_scale")
        f_div = sem("f_div")
        f_abs = sem("f_abs")
        f_grid = sem("f_grid")
        f_quant = sem("f_quant")
        f_xt = sem("f_xt")
        f_xt_copied = sem("f_xt_copied")
        f_gu = sem("f_gu")
        f_silu = sem("f_silu")
        f_h = sem("f_h")
        f_ht = sem("f_ht")
        f_ht_copied = sem("f_ht_copied")
        f_down = sem("f_down")
        f_out = sem("f_out")
        stored = sem("stored")

        x_rows = x_in[0].rearrange("(t p) d -> p t d", p=P)
        out_rows = out[0].rearrange("(t p) d -> p t d", p=P)
        wqkv_rows = w_qkv.rearrange("k (s g c) -> k s g c", s=3, c=P)

        def at(it, per_unit, w, plus=0):
            return it * (BODY * per_unit) + (w * per_unit + plus)

        def after(it, per_unit, w, plus=0):
            return at(it, per_unit, w, plus) + START

        def par(w):
            return (w // CHUNKS) % 2

        def pool_free(it, w, j):
            t = j - P_BUFS
            if t >= 0:
                return pool_adds, after(it, POOL_ADDS, w, max(t, 1))
            t += STEPS
            if t < POOL_TILES:
                return pool_adds, after(it, POOL_ADDS, w, t - POOL_ADDS)
            return dve_adds, at(it, DVE_ADDS, w, max(t - POOL_TILES, 1))

        def slot_of(n):
            return n // (2 * TQ), (n // TQ) % 2, n % TQ

        def by_block(a):
            return a.rearrange("p (b e) -> p b e", e=BLOCK)

        def each_block(a, n):
            return a.unsqueeze(2).to_broadcast([P, n, BLOCK])

        def quantised(n):
            kind, g = FF_ORDER[n]
            if kind == "x":
                return fx[:, g * NX:(g + 1) * NX], xq[:, g % 2, :], NX
            return hh[:, g % 2, :], hq[:, g % 2, :], NH

        def v_quarter(v, c):
            return v[:, c * TQ:(c + 1) * TQ, :].rearrange("p t d -> p (t d)")

        block = ctx.enter_context(nc.Block())

        @block.sync
        def _(sp):
            for g in range(GROUPS):
                sp.dma_start(y[:, g * TQ:(g + 1) * TQ, :], x_rows[:, g * TQ:(g + 1) * TQ, :]) \
                    .then_inc(x_loaded[g], 16)
            for pair in range(2):
                sp.dma_start(wqkv[pair][:, :, :], wqkv_rows[:, :, pair, :]).then_inc(wqkv_loaded[pair], 16)
            sp.dma_start(bias[:, :], b_out.partition_broadcast(P)).then_inc(bias_loaded, 16)
            sp.dma_start(wo[0][:, :], w_out[0:P, :]).then_inc(wo_loaded[0], 16)

            def body(it, last):
                for w in range(BODY):
                    pair = it * 2 + w // CHUNKS
                    if w % CHUNKS == 0 and not (last and w >= CHUNKS):
                        sp.wait_ge(misc_ready, misc_no(it, w, "proj", last) + 1)
                        sp.dma_start(wo[1 - par(w)][:, :], w_out[bass.ds((pair + 1) * P, P), :]) \
                            .then_inc(wo_loaded[1 - par(w)], 16)
                    if w % CHUNKS == 1 and not last:
                        sp.wait_ge(misc_ready, misc_no(it, w, "Q", last) + 1)
                        sp.dma_start(wqkv[par(w)][:, :, :],
                                     wqkv_rows[:, :, bass.ds(pair + 2, 1), :].rearrange("k s g c -> k (s g) c")) \
                            .then_inc(wqkv_loaded[par(w)], 16)

            with sp.Fori(0, ITERS - 1) as it:
                body(it, False)
            body(ITERS - 1, True)
            for g in range(GROUPS):
                sp.wait_ge(f_out, g + 1)
                sp.dma_start(out_rows[:, g * TQ:(g + 1) * TQ, :], y[:, g * TQ:(g + 1) * TQ, :]) \
                    .then_inc(stored, 16)
            sp.wait_ge(stored, 16 * GROUPS)

        @block.gpsimd
        def _(pool):
            count = {}

            def in_turn(ins, signal):
                count[signal] = count.get(signal, 0) + 1
                ins.then_inc(signal, 1)
                pool.wait_ge(signal, count[signal])

            in_turn(pool.memset(wx[64:P, 2 * DIM:3 * DIM], 0.0), wx_zeroed)
            in_turn(pool.memset(wx[64:P, 5 * DIM:6 * DIM], 0.0), wx_zeroed)
            for k, w in enumerate((w_gate, w_up)):
                pool.dma_start(wx[:, 3 * k * DIM:(3 * k + 2) * DIM].rearrange("p (t d) -> p t d", t=2),
                               w[0:2 * P, :].rearrange("(t p) d -> p t d", p=P)).then_inc(ffw_loaded, 16)
                pool.dma_start(wx[0:FF - 2 * P, (3 * k + 2) * DIM:(3 * k + 3) * DIM], w[2 * P:FF, :]) \
                    .then_inc(ffw_loaded, 16)
            pool.dma_start(wx[:, 6 * DIM:WX], w_down).then_inc(ffw_loaded, 16)
            in_turn(pool.memset(ident[:, :], 0.0), pool_step)
            in_turn(pool.affine_select(out=ident[:, :], in_=ident[:, :], compare_op=ALU.not_equal, fill=1.0,
                                       base=0, pattern=[[-1, P]], channel_multiplier=1), const_ready)
            in_turn(pool.memset(ones[:, :], 1.0), const_ready)
            for i in range(2):
                in_turn(pool.memset(kk[i][DH:P, :, 1, :].bitcast(F32), 0.0), pool_step)
                in_turn(pool.memset(kk[i][DH:DH + 1, :, 1, :].bitcast(F32), 1.0), zeros_ready)
            for i in range(Q_BUFS):
                in_turn(pool.memset(q2[i][DH:P, :, :].bitcast(F32), 0.0), zeros_ready)
            in_turn(pool.memset(o_raw[:, 1, :], 0.0), zeros_ready)
            in_turn(pool.memset(wo[1][:, :], 0.0), zeros_ready)

            nb = WX // BLOCK
            pool.wait_ge(wq_scale, 1)
            pool.tensor_tensor(by_block(wn), by_block(wx), each_block(binv[:, 0, 0:nb], nb), ALU.mult) \
                .then_inc(wq_div, 1)
            pool.sem_inc(pool_adds, START)
            pool.wait_ge(wq_grid, 1)
            pool.tensor_tensor(by_block(wx), by_block(wgrid), each_block(bscale[:, 0, 0:nb], nb), ALU.mult) \
                .then_inc(wq_done, 1)

            def body(it, last):
                for w in range(BODY):
                    acc = acc_pool[:, w % 2, :, :]
                    for j in range(1, POOL_TILES):
                        if j == 1:
                            pool.wait_ge(den_acc, after(it, 1, w))
                        else:
                            pool.wait_ge(pool_adds, after(it, POOL_ADDS, w, j - 1))
                        pool.wait_ge(p_ready, after(it, STEPS, w, j + 1))
                        first = probs[:, 0, :, :] if j == 1 else acc
                        pool.tensor_tensor(acc, first, probs[:, j % P_BUFS, :, :], ALU.add) \
                            .then_inc(pool_adds, 1)

            with pool.Fori(0, ITERS - 1) as it:
                body(it, False)
            body(ITERS - 1, True)

            for n in range(len(FF_ORDER) + 1):
                if n < len(FF_ORDER):
                    src, _dst, width = quantised(n)
                    nb = width // BLOCK
                    pool.wait_ge(f_scale, n + 1)
                    if n >= 2:
                        pool.wait_ge(f_abs, n - 1)
                    pool.tensor_tensor(by_block(scaled[:, n % 2, 0:width]), by_block(src),
                                       each_block(binv[:, n % 3, 0:nb], nb), ALU.mult).then_inc(f_div, 1)
                if n >= 1:
                    m = n - 1
                    kind, g = FF_ORDER[m]
                    _src, dst, width = quantised(m)
                    nb = width // BLOCK
                    pool.wait_ge(f_grid, m + 1)
                    if g >= 2:
                        pool.wait_ge(*((f_xt, g - 1) if kind == "x" else (f_ht, TQ * (g - 1))))
                    pool.tensor_tensor(by_block(dst), by_block(grid[:, m % 2, 0:width]),
                                       each_block(bscale[:, m % 3, 0:nb], nb), ALU.mult).then_inc(f_quant, 1)

        @block.scalar
        def _(act):
            def k_high(k, c, ps, h):
                return act.activation(k[0:DH, h, :, c * QC:(c + 1) * QC],
                                      ps[DH * h:DH * (h + 1), :].unsqueeze(1).to_broadcast([DH, 2, QC]), ACT.Copy)

            def q_high(q, ps, h, half):
                return act.activation(q[DH * half:DH * (half + 1), h, :], ps[DH * h:DH * (h + 1), :], ACT.Copy)

            def max_row(buf, count):
                act.wait_ge(maxrow_mm, count)
                act.activation(q2[buf][DH:DH + 1, :, :], mx_ps[DH:DH + 1, :, :], ACT.Copy).then_inc(maxrow_ready, 1)

            act.wait_ge(const_ready, 2)
            act.activation(ident_r[:, :], ident[:, :], ACT.Copy).then_inc(ident_r_ready, 1)
            act.wait_ge(var_ready, 1)
            act.activation(rs[:, 1, :], rs[:, 0, :], ACT.Sqrt).then_inc(root_ready, 1)
            for g in range(CHUNKS):
                act.wait_ge(xt_ready, g + 1)
                act.activation(xhat_t[:, g * QC:(g + 1) * QC], banks[g], ACT.Copy).then_inc(xt_copied, 1)
            for e in range(PRO_KQ):
                act.wait_ge(pro_mm, e + 1)
                ps = banks[PRO_BANKS[e]]
                if e < CHUNKS:
                    k_high(kk[0], e, ps, 0)
                    k_high(kk[0], e, ps, 1).then_inc(hi_done, 1)
                else:
                    q = q1[e - CHUNKS]
                    q_high(q, ps, 0, 0)
                    q_high(q, ps, 0, 1)
                    q_high(q, ps, 1, 0)
                    q_high(q, ps, 1, 1).then_inc(hi_done, 1)
            for c in range(CHUNKS):
                act.wait_ge(pro_mm, PRO_KQ + c + 1)
                act.activation(v_quarter(vv[0], c), banks[V_BANKS[c]], ACT.Copy).then_inc(pro_v, 1)
            act.sem_inc(p_ready, START)
            act.sem_inc(o_copied, START)
            act.wait_ge(wq_div, 1)
            act.activation(wa, wn, ACT.Abs).then_inc(wq_abs, 1)
            act.activation(wsign, wn, ACT.Sign).then_inc(wq_abs, 1)
            max_row(0, 1)
            act.wait_ge(wt_ready, 1)
            act.activation(wgu_t[:, 0:FF], banks[6][:, 0:FF], ACT.Copy).then_inc(wt_copied, 1)
            act.wait_ge(wt_ready, 2)
            act.activation(wgu_t[:, FF:2 * FF], banks[7][:, 0:FF], ACT.Copy).then_inc(wt_copied, 1)
            act.wait_ge(wt_ready, 3)
            for i, (_, rows) in enumerate(FF_TILES):
                act.activation(wd_t[0:rows, i, :], banks[6][0:rows, i * DIM:(i + 1) * DIM], ACT.Copy) \
                    .then_inc(wt_copied, 1)

            def body(it, last):
                for w in range(BODY):
                    for j in range(STEPS):
                        act.wait_ge(s_ready, at(it, STEPS, w, j + 1))
                        act.wait_ge(pv_done, at(it, STEPS, w, j + 1))
                        act.wait_ge(*pool_free(it, w, j))
                        act.activation(probs[:, j % P_BUFS, :, :], s_ps[:, j % 2, :, :], ACT.Exp, scale=SCALE) \
                            .then_inc(p_ready, 1)
                        if j in (6, 7) and not skipped("K", w, last):
                            act.wait_ge(misc_ready, misc_no(it, w, "K", last) + 1)
                            ins = k_high(kk[1 - par(w)], w % CHUNKS, misc_ps[:, :], j - 6)
                            if j == 7:
                                ins.then_inc(hi_done, 1)
                        if j == 10 and not skipped("V", w, last):
                            act.wait_ge(misc_ready, misc_no(it, w, "V", last) + 1)
                            act.activation(v_quarter(vv[1 - par(w)], w % CHUNKS), misc_ps[:, :], ACT.Copy) \
                                .then_inc(misc_free, 1)
                        if j in (11, 12, 13, 14) and not skipped("Q", w, last):
                            act.wait_ge(misc_ready, misc_no(it, w, "Q", last) + 1)
                            ins = q_high(q1[(w + 2) % Q_BUFS], misc_ps[:, :], (j - 11) // 2, (j - 11) % 2)
                            if j == 14:
                                ins.then_inc(hi_done, 1)
                    if not (last and w == BODY - 1):
                        max_row((w + 1) % Q_BUFS, at(it, 1, w, 2))
                    act.wait_ge(pv_done, at(it, STEPS, w, STEPS + P_BUFS))
                    act.wait_ge(o_normed, after(it, 1, w))
                    act.activation(o_raw[:, w % 2, :], o_ps[:, :], ACT.Copy).then_inc(o_copied, 1)

            with act.Fori(0, ITERS - 1) as it:
                body(it, False)
            body(ITERS - 1, True)

            act.wait_ge(var_ready, 2)
            act.activation(rs[:, 1, :], rs[:, 0, :], ACT.Sqrt).then_inc(root_ready, 1)
            for what, n in ACT_ORDER:
                if what == "abs":
                    width = quantised(n)[2]
                    act.wait_ge(f_div, n + 1)
                    if n >= 2:
                        act.wait_ge(f_grid, n - 1)
                    act.activation(size[:, n % 2, 0:width], scaled[:, n % 2, 0:width], ACT.Abs)
                    act.activation(sign[:, n % 2, 0:width], scaled[:, n % 2, 0:width], ACT.Sign).then_inc(f_abs, 1)
                elif what == "T":
                    act.wait_ge(f_xt, n + 1)
                    if n >= 2:
                        act.wait_ge(f_gu, TQ * (n - 1))
                    act.activation(xq_t[:, n % 2, :], banks[4], ACT.Copy).then_inc(f_xt_copied, 1)
                elif what == "silu":
                    for k in range(TQ * n, TQ * (n + 1)):
                        act.wait_ge(f_gu, k + 1)
                        if k >= 2:
                            act.wait_ge(f_h, k - 1)
                        act.activation(silu[:, k % 2, :], banks[2 * (k % 2)][:, 0:FF], ACT.Silu) \
                            .then_inc(f_silu, 1)
                else:
                    for k in range(TQ * n, TQ * (n + 1)):
                        act.wait_ge(f_ht, k + 1)
                        if k >= 2:
                            act.wait_ge(f_down, k - 1)
                        for i, (_, rows) in enumerate(FF_TILES):
                            ins = act.activation(hq_t[0:rows, k % 2, i, :],
                                                 banks[5 + k % 2][0:rows, i * P:(i + 1) * P], ACT.Copy)
                        ins.then_inc(f_ht_copied, 1)

        @block.vector
        def _(dve):
            step = [0]

            def inc(ins):
                step[0] += 1
                ins.then_inc(dve_step, 1)

            def settle():
                dve.wait_ge(dve_step, step[0])

            def layer_stats(t):
                inc(dve.bn_stats(stats[:, t, :], y[:, t, :]))

            def inverse_root(n):
                settle()
                for t in range(N // P):
                    inc(dve.bn_aggr(mv[:, t, :], stats[:, t, :]))
                settle()
                dve.tensor_scalar(rs[:, 0, :], mv[:, :, 1], EPS, None, ALU.add).then_inc(var_ready, 1)
                dve.wait_ge(root_ready, n)
                inc(dve.reciprocal(rs[:, 2, :], rs[:, 1, :]))
                settle()
                inc(dve.tensor_tensor(rs[:, 3, :], rs[:, 0, :], rs[:, 2, :], ALU.mult))
                settle()
                inc(dve.tensor_tensor(rs[:, 2, :], rs[:, 3, :], rs[:, 1, :], ALU.add))
                settle()
                inc(dve.tensor_scalar(rs[:, 1, :], rs[:, 2, :], 0.5, None, ALU.mult))
                settle()
                inc(dve.reciprocal(rs[:, 3, :], rs[:, 1, :]))
                settle()

            def normed(dst, t):
                return dve.tensor_scalar(dst[:, t * DIM:(t + 1) * DIM], y[:, t, :], mv[:, t, 0:1],
                                         rs[:, 3, t:t + 1], ALU.subtract, ALU.mult)

            def grid_value(value, sgn, g2):
                inc(dve.tensor_scalar(g2, value, THRESHOLDS[6], 2.0, ALU.is_gt, ALU.mult))
                for m in (THRESHOLDS[5], THRESHOLDS[4]):
                    settle()
                    inc(dve.scalar_tensor_tensor(g2, value, m, g2, ALU.is_gt, ALU.add))
                settle()
                inc(dve.tensor_scalar(g2, g2, 2.0, None, ALU.mult))
                for m in THRESHOLDS[0:4]:
                    settle()
                    inc(dve.scalar_tensor_tensor(g2, value, m, g2, ALU.is_gt, ALU.add))
                settle()
                return dve.scalar_tensor_tensor(g2, g2, 0.5, sgn, ALU.mult, ALU.mult)

            def block_scales(src, nb, b):
                inc(dve.tensor_reduce(amax[:, 0:nb], by_block(src), AX.X, ALU.max, apply_absolute_value=True))
                settle()
                inc(dve.tensor_scalar(bscale[:, b, 0:nb], amax[:, 0:nb], 1.0 / 6.0, 1e-12, ALU.mult, ALU.max))
                settle()
                return dve.reciprocal(binv[:, b, 0:nb], bscale[:, b, 0:nb])

            def k_low(k, c, ps, h):
                cols = slice(c * QC, (c + 1) * QC)
                return dve.tensor_tensor(k[DH:P, h, 0, cols], ps[DH * h:DH * (h + 1), :],
                                         k[0:DH, h, 0, cols].bitcast(F32), ALU.subtract)

            def q_low(buf, ps, h):
                return dve.tensor_tensor(q2[buf][0:DH, h, :], ps[DH * h:DH * (h + 1), :],
                                         q1[buf][0:DH, h, :].bitcast(F32), ALU.subtract)

            def max_slot(n, count):
                dve.wait_ge(mx_ready, count)
                dve.tensor_reduce(part_max[:, n:n + 1], mx_ps[:, n % 2, :], AX.X, ALU.max).then_inc(mx_free, 1)

            def neg_maximum(count):
                dve.wait_ge(mx_free, count)
                dve.tensor_reduce(neg_max[:, :], part_max[:, :].rearrange("p (k n) -> p n k", k=CHUNKS),
                                  AX.X, ALU.max, negate=True).then_inc(negmax_ready, 1)

            def invert(it, w, last, t):
                cols = slice(t * P, (t + 1) * P)
                dve.wait_ge(misc_ready, misc_no(it, w, "den", last) + 1)
                ins = dve.reciprocal(rden[:, cols], misc_ps[:, cols])
                if t == TQ - 1:
                    ins.then_inc(misc_free, 1)

            def normalise(it, w, last):
                dve.wait_ge(misc_free, misc_no(it, w, "den", last) + START + 1)
                dve.wait_ge(o_copied, after(it, 1, w))
                dve.tensor_tensor(o_norm[:, :], o_raw[:, (w - 1) % 2, :], rden[:, :], ALU.mult).then_inc(o_normed, 1)

            def add_projection(it, w, last):
                c = (w - 1) % CHUNKS
                yc = y[:, c * TQ:(c + 1) * TQ, :]
                dve.wait_ge(misc_ready, misc_no(it, w, "proj", last) + 1)
                dve.tensor_tensor(yc, yc, misc_ps[:, :].rearrange("p (t d) -> p t d", t=TQ), ALU.add) \
                    .then_inc(misc_free, 1)

            for t in range(N // P):
                if t % TQ == 0:
                    dve.wait_ge(x_loaded[t // TQ], 16)
                layer_stats(t)
            inverse_root(1)
            for t in range(N // P):
                normed(xhat, t).then_inc(xhat_ready, 1)
            dve.wait_ge(ffw_loaded, 80)
            block_scales(wx, WX // BLOCK, 0).then_inc(wq_scale, 1)
            dve.wait_ge(bias_loaded, 16)
            inc(dve.tensor_tensor(y[:, :, :], y[:, :, :],
                                  bias[:, :].unsqueeze(1).to_broadcast([P, N // P, DIM]), ALU.add))
            dve.wait_ge(zeros_ready, 4 + Q_BUFS)
            for e in range(PRO_KQ):
                dve.wait_ge(hi_done, e + 1)
                ps = banks[PRO_BANKS[e]]
                if e < CHUNKS:
                    k_low(kk[0], e, ps, 0)
                    k_low(kk[0], e, ps, 1).then_inc(pro_lo, 1)
                else:
                    q_low(e - CHUNKS, ps, 0)
                    q_low(e - CHUNKS, ps, 1).then_inc(pro_lo, 1)
            dve.wait_ge(xt_ready, CHUNKS)
            dve.memset(acc_dve[:, 1, 0, :], 1.0).then_inc(den_acc, 1)
            dve.memset(acc_dve[:, 1, 1, :], 1.0).then_inc(dve_adds, DVE_ADDS)
            dve.sem_inc(den_acc, START)
            dve.sem_inc(o_normed, START)
            dve.sem_inc(misc_free, START)
            for n in range(SLOTS):
                max_slot(n, n + 1)
                if n == SLOTS // 2:
                    dve.wait_ge(wq_abs, 2)
                    grid_value(wa, wsign, wgrid).then_inc(wq_grid, 1)
            neg_maximum(SLOTS)

            def body(it, last):
                for w in range(BODY):
                    ahead = not (last and w == BODY - 1)
                    sums = acc_dve[:, w % 2, :, :]
                    for j in range(STEPS):
                        if ahead:
                            for n in range(sum(SLOTS_AT[:j]), sum(SLOTS_AT[:j + 1])):
                                max_slot(n, at(it, SLOTS, w + 1, n + 1))
                            if j == 14:
                                neg_maximum(at(it, SLOTS, w + 2))
                        if 1 <= j <= TQ:
                            invert(it, w, last, j - 1)
                        if j == 5:
                            normalise(it, w, last)
                        if j == 7 and not skipped("K", w, last):
                            dve.wait_ge(hi_done, kq_no(it, w, "K", last))
                            k_low(kk[1 - par(w)], w % CHUNKS, misc_ps[:, :], 0)
                            k_low(kk[1 - par(w)], w % CHUNKS, misc_ps[:, :], 1).then_inc(misc_free, 1)
                        if j == 8:
                            add_projection(it, w, last)
                        if j == 15 and not skipped("Q", w, last):
                            dve.wait_ge(hi_done, kq_no(it, w, "Q", last))
                            q_low((w + 2) % Q_BUFS, misc_ps[:, :], 0)
                            q_low((w + 2) % Q_BUFS, misc_ps[:, :], 1).then_inc(misc_free, 1)
                        if j == POOL_TILES + 1:
                            dve.wait_ge(p_ready, after(it, STEPS, w, j + 1))
                            dve.tensor_tensor(sums, probs[:, (j - 1) % P_BUFS, :, :], probs[:, j % P_BUFS, :, :],
                                              ALU.add).then_inc(dve_adds, 1)
                        if j > POOL_TILES + 1:
                            dve.wait_ge(p_ready, after(it, STEPS, w, j + 1))
                            dve.wait_ge(dve_adds, at(it, DVE_ADDS, w, j - POOL_TILES - 1 + DVE_ADDS))
                            dve.tensor_tensor(sums, sums, probs[:, j % P_BUFS, :, :], ALU.add).then_inc(dve_adds, 1)
                    dve.wait_ge(pool_adds, after(it, POOL_ADDS, w, POOL_ADDS))
                    dve.wait_ge(dve_adds, at(it, DVE_ADDS, w, 2 * DVE_ADDS))
                    dve.tensor_tensor(sums, sums, acc_pool[:, w % 2, :, :], ALU.add).then_inc(den_acc, 1)

            with dve.Fori(0, ITERS - 1) as it:
                body(it, False)
            body(ITERS - 1, True)
            for t in range(TQ):
                invert(ITERS - 1, BODY, True, t)
            normalise(ITERS - 1, BODY, True)
            add_projection(ITERS - 1, BODY, True)

            def finish(g):
                yg = y[:, g * TQ:(g + 1) * TQ, :]
                dve.wait_ge(f_down, TQ * (g + 1))
                dve.tensor_tensor(yg, yg, banks[7].rearrange("p (t d) -> p t d", t=TQ), ALU.add).then_inc(f_out, 1)

            dve.wait_ge(misc_free, misc_no(ITERS - 1, BODY, "proj", True) + START + 1)
            for t in range(N // P):
                layer_stats(t)
            inverse_root(2)
            for t in range(N // P):
                inc(normed(fx, t))
            settle()
            for n in range(len(FF_ORDER) + 1):
                if n in FINISH_BEFORE:
                    finish(FINISH_BEFORE[n])
                if n < len(FF_ORDER):
                    kind, g = FF_ORDER[n]
                    src, _dst, width = quantised(n)
                    if kind == "h":
                        for k in range(TQ * g, TQ * (g + 1)):
                            dve.wait_ge(f_silu, k + 1)
                            dve.tensor_tensor(src[:, (k % TQ) * FF:(k % TQ + 1) * FF], silu[:, k % 2, :],
                                              banks[2 * (k % 2) + 1][:, 0:FF], ALU.mult).then_inc(f_h, 1)
                        dve.wait_ge(f_h, TQ * (g + 1))
                    if n >= 3:
                        dve.wait_ge(f_quant, n - 2)
                    block_scales(src, width // BLOCK, n % 3).then_inc(f_scale, 1)
                if n >= 1:
                    m = n - 1
                    width = quantised(m)[2]
                    dve.wait_ge(f_abs, m + 1)
                    if m >= 2:
                        dve.wait_ge(f_quant, m - 1)
                    grid_value(size[:, m % 2, 0:width], sign[:, m % 2, 0:width], grid[:, m % 2, 0:width]) \
                        .then_inc(f_grid, 1)
            finish(FINISH_BEFORE[len(FF_ORDER) + 1])
            finish(GROUPS - 1)

        @block.tensor
        def _(pe):
            def project(ps, weights, c):
                return pe.matmul(ps, weights, xhat_t[:, c * QC:(c + 1) * QC], start=True, stop=True)

            def project_v(ps, weights, c):
                for t in range(TQ):
                    row = (c * TQ + t) * P
                    ins = pe.matmul(ps[:, t * P:(t + 1) * P], xhat_t[:, row:row + P], weights, start=True, stop=True)
                return ins

            def scores(buf, k, q, j):
                keys = slice(j * P, (j + 1) * P)
                for h in range(2):
                    pe.matmul(s_ps[:, buf, h, :], k[:, h, 0, keys], q1[q][:, h, :], start=True, stop=False)
                for h in range(2):
                    ins = pe.matmul(s_ps[:, buf, h, :], k[:, h, 1, keys], q2[q][:, h, :], start=False, stop=True)
                return ins

            def max_scores(n, k, q):
                kq, h, t = slot_of(n)
                return pe.matmul(mx_ps[:, n % 2, :], q1[q][:, h, t * P:(t + 1) * P],
                                 k[:, h, 0, kq * QC:(kq + 1) * QC], start=True, stop=True)

            def max_rows():
                for i in range(2 * TQ):
                    ins = pe.matmul(mx_ps[:, i // TQ, (i % TQ) * P:(i % TQ + 1) * P],
                                    neg_max[:, i:i + 1].to_broadcast([P, P]), ident_r[:, :], start=True, stop=True)
                return ins

            pe.wait_ge(const_ready, 2)
            for g in range(CHUNKS):
                pe.wait_ge(xhat_ready, TQ * (g + 1))
                for t in range(TQ):
                    row = (g * TQ + t) * DIM
                    ins = pe.transpose(banks[g][:, t * P:(t + 1) * P], xhat[:, row:row + DIM], ident[:, :])
                ins.then_inc(xt_ready, 1)
            pe.wait_ge(wqkv_loaded[0], 16)
            for e in range(PRO_KQ):
                pe.wait_ge(xt_copied, min(e + 1, CHUNKS))
                project(banks[PRO_BANKS[e]], wqkv[0][:, 1 if e < CHUNKS else 0, :], e % CHUNKS).then_inc(pro_mm, 1)
            for c in range(CHUNKS):
                if c >= 2:
                    pe.wait_ge(pro_v, c - 1)
                project_v(banks[V_BANKS[c]], wqkv[0][:, 2, :], c).then_inc(pro_mm, 1)
            pe.wait_ge(pro_lo, PRO_KQ)
            for n in range(SLOTS):
                if n >= 2:
                    pe.wait_ge(mx_free, n - 1)
                max_scores(n, kk[0], 0).then_inc(mx_ready, 1)
            pe.wait_ge(ident_r_ready, 1)
            pe.wait_ge(negmax_ready, 1)
            max_rows().then_inc(maxrow_mm, 1)
            pe.wait_ge(wq_done, 1)
            pe.wait_ge(pro_v, CHUNKS)
            for k in range(2):
                for i, (row, rows) in enumerate(FF_TILES):
                    ins = pe.transpose(banks[6 + k][:, row:row + rows], wx[0:rows, (3 * k + i) * DIM:(3 * k + i + 1) * DIM],
                                       ident[0:rows, 0:rows])
                ins.then_inc(wt_ready, 1)
            pe.wait_ge(wt_copied, 1)
            for i, (row, rows) in enumerate(FF_TILES):
                ins = pe.transpose(banks[6][0:rows, i * DIM:(i + 1) * DIM], wx[:, 6 * DIM + row:6 * DIM + row + rows],
                                   ident[:, :])
            ins.then_inc(wt_ready, 1)
            pe.wait_ge(maxrow_ready, 1)
            scores(0, kk[0], 0, 0).then_inc(s_ready, 1)
            pe.wait_ge(wt_copied, 2 + len(FF_TILES))
            max_scores(0, kk[0], 0).then_inc(pv_done, P_BUFS)

            def misc(name, it, w, last):
                c = w % CHUNKS
                pe.wait_ge(misc_free, misc_no(it, w, name, last) + START)
                ps = misc_ps[:, :]
                if name == "K":
                    if c == 0:
                        pe.wait_ge(wqkv_loaded[1 - par(w)], it * 16 + (w // CHUNKS + 1) * 16)
                    ins = project(ps, wqkv[1 - par(w)][:, 1, :], c)
                elif name == "V":
                    ins = project_v(ps, wqkv[1 - par(w)][:, 2, :], c)
                elif name == "Q":
                    ins = project(ps, wqkv[par(w + 2)][:, 0, :], (w + 2) % CHUNKS)
                elif name == "den":
                    pe.wait_ge(den_acc, after(it, 1, w, 1))
                    for h in range(2):
                        ins = pe.matmul(ps[DH * h:DH * (h + 1), :], ones[:, :], acc_dve[:, (w - 1) % 2, h, :],
                                        start=True, stop=True)
                else:
                    if c == 1:
                        pe.wait_ge(wo_loaded[par(w)], it * 16 + 16)
                    pe.wait_ge(o_normed, after(it, 1, w, 1))
                    for t in range(TQ):
                        ins = pe.matmul(ps[:, t * P:(t + 1) * P], o_norm[:, t * P:(t + 1) * P], wo[par(w - 1)][:, :],
                                        start=True, stop=True)
                ins.then_inc(misc_ready, 1)

            def weighted(it, w, j):
                pe.wait_ge(p_ready, after(it, STEPS, w, j + 1))
                if j == 0:
                    pe.wait_ge(o_copied, after(it, 1, w))
                for h in range(2):
                    ins = pe.matmul(o_ps[DH * h:DH * (h + 1), :], vv[par(w)][:, j, DH * h:DH * (h + 1)],
                                    probs[:, j % P_BUFS, h, :], start=(j == 0), stop=(j == STEPS - 1))
                ins.then_inc(pv_done, 1)

            def body(it, last):
                for w in range(BODY):
                    ahead = not (last and w == BODY - 1)
                    pe.wait_ge(misc_free, misc_before(it, w, last) + START)
                    for j in range(STEPS):
                        if j < STEPS - 1:
                            pe.wait_ge(p_ready, after(it, STEPS, w, j))
                            scores((j + 1) % 2, kk[par(w)], w % Q_BUFS, j + 1).then_inc(s_ready, 1)
                        slots = list(range(sum(SLOTS_AT[:j]), sum(SLOTS_AT[:j + 1]))) if ahead else []

                        def row_maxima(slots):
                            for n in slots:
                                pe.wait_ge(mx_free, at(it, SLOTS, w + 1, n - 1))
                                if w % CHUNKS == CHUNKS - 1 and n == SLOTS - 2 * TQ:
                                    if not skipped("K", w, last):
                                        pe.wait_ge(misc_free, misc_no(it, w, "K", last) + START + 1)
                                max_scores(n, kk[par(w + 1)], (w + 1) % Q_BUFS).then_inc(mx_ready, 1)
                        row_maxima(slots[:2])
                        if j in MISC_AT and not skipped(MISC_AT[j], w, last):
                            misc(MISC_AT[j], it, w, last)
                        weighted(it, w, j)
                        row_maxima(slots[2:])
                        if j == STEPS - 2 and ahead:
                            pe.wait_ge(negmax_ready, at(it, 1, w, 2))
                            max_rows().then_inc(maxrow_mm, 1)
                        if j == STEPS - 1 and ahead:
                            pe.wait_ge(maxrow_ready, at(it, 1, w, 2))
                            pe.wait_ge(p_ready, after(it, STEPS, w, j))
                            scores(0, kk[par(w + 1)], (w + 1) % Q_BUFS, 0).then_inc(s_ready, 1)

            with pe.Fori(0, ITERS - 1) as it:
                body(it, False)
            body(ITERS - 1, True)
            misc("den", ITERS - 1, BODY, True)
            misc("proj", ITERS - 1, BODY, True)

            def transpose_h(k, g):
                if k >= 2:
                    pe.wait_ge(f_ht_copied, k - 1)
                for i, (col, rows) in enumerate(FF_TILES):
                    start = (k % TQ) * FF + col
                    ins = pe.transpose(banks[5 + k % 2][0:rows, i * P:(i + 1) * P], hq[:, g % 2, start:start + rows],
                                       ident[:, :])
                ins.then_inc(f_ht, 1)

            def down(k):
                pe.wait_ge(f_ht_copied, k + 1)
                for i, (_, rows) in enumerate(FF_TILES):
                    ins = pe.matmul(banks[7][:, (k % TQ) * DIM:(k % TQ + 1) * DIM], hq_t[0:rows, k % 2, i, :],
                                    wd_t[0:rows, i, :], start=(i == 0), stop=(i == len(FF_TILES) - 1))
                ins.then_inc(f_down, 1)

            pe.wait_ge(misc_free, misc_no(ITERS - 1, BODY, "proj", True) + START + 1)
            for what, g in PE_ORDER:
                if what == "T":
                    pe.wait_ge(f_quant, FF_ORDER.index(("x", g)) + 1)
                    if g:
                        pe.wait_ge(f_xt_copied, g)
                    for t in range(TQ):
                        ins = pe.transpose(banks[4][:, t * P:(t + 1) * P], xq[:, g % 2, t * DIM:(t + 1) * DIM],
                                           ident[:, :])
                    ins.then_inc(f_xt, 1)
                elif what == "gu":
                    pe.wait_ge(f_xt_copied, g + 1)
                    for k in range(TQ * g, TQ * (g + 1)):
                        if k >= 2:
                            pe.wait_ge(f_h, k - 1)
                        for i in range(2):
                            ins = pe.matmul(banks[2 * (k % 2) + i][:, 0:FF], xq_t[:, g % 2, (k % TQ) * P:(k % TQ + 1) * P],
                                            wgu_t[:, i * FF:(i + 1) * FF], start=True, stop=True)
                        ins.then_inc(f_gu, 1)
                else:
                    pe.wait_ge(f_quant, FF_ORDER.index(("h", g)) + 1)
                    if g:
                        pe.wait_ge(f_out, g)
                    transpose_h(TQ * g, g)
                    for k in range(TQ * g, TQ * (g + 1)):
                        if k + 1 < TQ * (g + 1):
                            transpose_h(k + 1, g)
                        down(k)


_INS = ["L0_attn_x", "L0_attn_w_qkv", "L0_attn_w_out", "L0_attn_b_out", "L0_ffn_w_gate", "L0_ffn_w_up",
        "L0_ffn_w_down"]


def kernel(**inputs):
    import concourse.bacc as bacc
    from concourse.bass_utils import run_bass_kernel_spmd

    nc = bacc.Bacc("TRN2", target_bir_lowering=False, num_devices=1)
    arrays, args = {}, []
    for name in _INS:
        a = np.ascontiguousarray(inputs[name])
        arrays[f"in_{name}"] = a
        args.append(nc.dram_tensor(f"in_{name}", a.shape, mybir.dt.from_np(a.dtype), kind="ExternalInput").ap())
    out = nc.dram_tensor("out", (1, N, DIM), F32, kind="ExternalOutput").ap()
    block_kernel(nc, *args, out)
    return run_bass_kernel_spmd(nc, [arrays], core_ids=[0]).results[0]["out"]
```
